# Optimizing a Trainium2 kernel written in Bass

```python
import numpy as np
import jax
import jax.numpy as jnp

def _softmax(x, axis=-1):
    return jax.nn.softmax(x, axis=axis)

def _gelu(x):
    return jax.nn.gelu(x, approximate=True)

def _silu(x):
    return jax.nn.silu(x)

def _sigmoid(x):
    return jax.nn.sigmoid(x)

def _layernorm(x, axis=-1, eps=1e-05):
    m = jnp.mean(x, axis=axis, keepdims=True)
    v = jnp.var(x, axis=axis, keepdims=True)
    return (x - m) / jnp.sqrt(v + eps)

def _scatter_add(tgt, idx, src, axis=0):
    return tgt.at[idx].add(src)

def _segment_sum(src, seg, n):
    return jax.ops.segment_sum(src, seg, n)
kernel_name = 'mk_flamingo_gated_d1_seqx_r8_d7b428'

def setup_inputs(seed: int=0):
    np.random.seed(seed)
    _w = jnp.asarray

    def _rec_inputs():
        import jax
        import jax.numpy as jnp
        _rk = jax.random.key(seed)
        x = -0.0003929 + 0.9999 * jax.random.normal(jax.random.fold_in(_rk, 1), (64, 64, 128), jnp.float32)
        _lenS = 64 - jax.random.randint(jax.random.fold_in(_rk, 7), (64,), 0, max(1, 64 // 4) + 1, jnp.int32)
        _lenS2 = 64 - jax.random.randint(jax.random.fold_in(_rk, 8), (64,), 0, max(1, 64 // 4) + 1, jnp.int32)
        _ctx_1024P = jax.random.normal(jax.random.fold_in(_rk, 11), (64, 16, 128), jnp.float32)
        _ctx_1024c = jax.random.dirichlet(jax.random.fold_in(_rk, 511), 0.3 * jnp.ones((16,), jnp.float32), (64, 64))
        _ctx_1024t = jnp.einsum('bsk,bkd->bsd', _ctx_1024c, _ctx_1024P)
        _ctx_1024t = _ctx_1024t * jax.lax.rsqrt(jnp.mean(jnp.square(_ctx_1024t)) + 1e-12) * 0.953939
        ctx_1024 = 2.81802e-05 + 1.00001 * (_ctx_1024t + 0.3 * jax.random.normal(jax.random.fold_in(_rk, 611), (64, 64, 128), jnp.float32))
        _g = jax.random.normal(jax.random.fold_in(_rk, 9001), (2, 1), jnp.float32)
        _g = jnp.sign(_g) * jnp.maximum(jnp.abs(_g), 1.0) + (_g == 0) * 1.0
        g_xattn = _g[0]
        g_ffn = _g[1]
        return (x, ctx_1024, g_xattn, g_ffn)
    x, ctx_1024, g_xattn, g_ffn = _rec_inputs()

    def _L0_xattn_setup():
        import jax, jax.numpy as jnp
        import numpy as np
        B, T, D = (8, 256, 128)
        key = jax.random.key(seed)
        kq, kk, kv = jax.random.split(key, 3)
        return {'query': jax.random.normal(kq, (B, T, D), dtype=jnp.float32), 'key': jax.random.normal(kk, (B, T, D), dtype=jnp.float32), 'value': jax.random.normal(kv, (B, T, D), dtype=jnp.float32)}
    _L0_xattn_all = _L0_xattn_setup()
    _L0_xattn_in = {k: v for k, v in _L0_xattn_all.items() if k in ()}
    del _L0_xattn_all

    def _L0_ffn_setup():
        import jax, jax.numpy as jnp
        import numpy as np
        DIM = 128
        HIDDEN = 384
        SCALE = 1.0 / 127.0

        def _dequant(w_int, dtype):
            return w_int.astype(dtype) * jnp.asarray(SCALE, dtype)
        key = jax.random.key(seed)
        k_x, k_g, k_u, k_d = jax.random.split(key, 4)
        x = jax.random.normal(k_x, (4, 256, DIM), dtype=jnp.float32)
        w_gate = jax.random.randint(k_g, (HIDDEN, DIM), -127, 128, dtype=jnp.int32)
        w_up = jax.random.randint(k_u, (HIDDEN, DIM), -127, 128, dtype=jnp.int32)
        w_down = jax.random.randint(k_d, (DIM, HIDDEN), -127, 128, dtype=jnp.int32)
        return {'x': x, 'w_gate': w_gate, 'w_up': w_up, 'w_down': w_down}
    _L0_ffn_all = _L0_ffn_setup()
    _L0_ffn_in = {k: v for k, v in _L0_ffn_all.items() if k in ('w_gate', 'w_up', 'w_down')}
    del _L0_ffn_all
    return {'x': x, 'ctx_1024': ctx_1024, 'g_xattn': g_xattn, 'g_ffn': g_ffn, 'L0_ffn_w_gate': _L0_ffn_in['w_gate'], 'L0_ffn_w_up': _L0_ffn_in['w_up'], 'L0_ffn_w_down': _L0_ffn_in['w_down']}

def reference(x, ctx_1024, g_xattn, g_ffn, L0_ffn_w_gate, L0_ffn_w_up, L0_ffn_w_down):
    import jax
    import jax.numpy as jnp

    def _L0_xattn_ref(query, key, value):
        import jax, jax.numpy as jnp
        import numpy as np
        B, T, D = (8, 256, 128)
        d = query.shape[-1]
        scores = jnp.einsum('bqd,bkd->bqk', query, key) * d ** (-0.5)
        tril = jnp.tril(jnp.ones((query.shape[1], key.shape[1]), dtype=bool))
        scores = jnp.where(tril, scores, -jnp.inf)
        attn = jax.nn.softmax(scores, axis=-1)
        return jnp.einsum('bqk,bkd->bqd', attn, value)

    def _L0_ffn_ref(x, w_gate, w_up, w_down):
        import jax, jax.numpy as jnp
        import numpy as np
        DIM = 128
        HIDDEN = 384
        SCALE = 1.0 / 127.0

        def _dequant(w_int, dtype):
            return w_int.astype(dtype) * jnp.asarray(SCALE, dtype)
        wg = _dequant(w_gate, x.dtype)
        wu = _dequant(w_up, x.dtype)
        wd = _dequant(w_down, x.dtype)
        gate = jnp.einsum('bsd,hd->bsh', x, wg)
        up = jnp.einsum('bsd,hd->bsh', x, wu)
        h = jax.nn.silu(gate) * up
        return jnp.einsum('bsh,dh->bsd', h, wd)
    x = x + jnp.tanh(g_xattn[0]) * _L0_xattn_ref(_layernorm(x, axis=-1), ctx_1024, ctx_1024)
    x = x + jnp.tanh(g_ffn[0]) * _L0_ffn_ref(_layernorm(x, axis=-1), L0_ffn_w_gate, L0_ffn_w_up, L0_ffn_w_down)
    return x

_drawn_inputs = setup_inputs


def setup_inputs(seed=0):
    import zlib

    import numpy as np

    out = dict(_drawn_inputs(seed))
    spreads = {}
    factors = {}
    for name, (base, spread) in spreads.items():
        noise = np.random.default_rng([zlib.crc32(name.encode()), seed]).standard_normal(out[name].shape)
        drawn = base * np.exp(spread * noise) if base else spread * noise
        out[name] = jnp.asarray(drawn.astype(out[name].dtype))
    for name, factor in factors.items():
        out[name] = (out[name] * factor).astype(out[name].dtype)
    return out
```

```python
from contextlib import ExitStack

import concourse.bass as bass
from concourse import mybir

F32 = mybir.dt.float32
F32R = mybir.dt.float32r
BF16 = mybir.dt.bfloat16
I32 = mybir.dt.int32
ALU = mybir.AluOpType
ACT = mybir.ActivationFunctionType
AX_X = mybir.AxisListType.X

P = 128
EPS = 1e-5
WEIGHT_SCALE = 1.0 / 127.0
MASKED = -1e30
TILES = 4
ROWS = TILES * P
HID = 3


def build(nc, x, ctx, g_xattn, g_ffn, w_gate, w_up, w_down, out):
    B, S, D = x.shape
    H = w_gate.shape[0]
    assert D == P and S == P // 2 and H == HID * P and (B * S) % ROWS == 0
    CHUNKS = B * S // ROWS
    LOOP = (1, CHUNKS - 3)
    SCORE_SCALE = float(D) ** -0.5

    x_rows = x.rearrange("b s d -> (b s) d").rearrange("(c t p) d -> c p t d", t=TILES, p=P)
    out_rows = out.rearrange("b s d -> (b s) d").rearrange("(c t p) d -> c p t d", t=TILES, p=P)
    ctx_rows = ctx.rearrange("(c u gh) s d -> c u s gh d", u=2, gh=4)

    with ExitStack() as stack:
        def sb(name, shape, dt=F32):
            return stack.enter_context(nc.sbuf_tensor(name, shape, dt))

        def psum(name):
            return stack.enter_context(nc.psum_tensor(name, [P, 512], F32))

        def sem(name):
            return stack.enter_context(nc.semaphore(name))

        x_norm_in = sb("x_norm_in", [P, TILES, D])
        x_resid = sb("x_resid", [P, TILES, D])
        ctx_keys = sb("ctx_keys", [P, 4, D])
        ctx_values = sb("ctx_values", [P, 4, D])
        ident = sb("ident", [P, P])
        ident_bf = sb("ident_bf", [P, P], BF16)
        mask = sb("mask", [P, TILES, S], BF16)
        minus_half = sb("minus_half", [P, TILES])
        gates_in = sb("gates_in", [P, 2])
        gates = sb("gates", [P, 2])
        down_scale = sb("down_scale", [P, 1])
        carrier = sb("carrier", [P, 2])
        w_int = sb("w_int", [P, 3, H], I32)
        w_nat = sb("w_nat", [P, 3, H])
        wg = sb("wg", [P, H], F32R)
        wu = sb("wu", [P, H], F32R)
        wd = sb("wd", [P, HID, D])
        bn1 = sb("bn1", [P, TILES, 6])
        mom1 = sb("mom1", [P, TILES, 2])
        negmean1 = sb("negmean1", [P, TILES])
        vareps1 = sb("vareps1", [P, TILES])
        rstd1 = sb("rstd1", [P, TILES])
        xn = sb("xn", [P, TILES, D])
        xnT = sb("xnT", [P, ROWS])
        ctxT = sb("ctxT", [P, ROWS])
        rowmax = sb("rowmax", [P, TILES])
        shifted = sb("shifted", [P, TILES, S])
        probs = sb("probs", [P, TILES, S])
        rowsum = sb("rowsum", [P, TILES])
        rrec = sb("rrec", [P, TILES])
        coef = sb("coef", [P, TILES])
        probsT = sb("probsT", [P, 2 * P])
        attn = sb("attn", [P, TILES, D])
        x1 = sb("x1", [P, CHUNKS, TILES, D])
        bn2 = sb("bn2", [P, TILES, 6])
        mom2 = sb("mom2", [P, TILES, 2])
        negmean2 = sb("negmean2", [P, TILES])
        vareps2 = sb("vareps2", [P, TILES])
        rstd2 = sb("rstd2", [P, TILES])
        shift2 = sb("shift2", [P, TILES])
        x1n = sb("x1n", [P, TILES, D])
        x1T_hi = sb("x1T_hi", [P, ROWS], F32R)
        x1T_lo = sb("x1T_lo", [P, ROWS], F32R)
        tanh_g = sb("tanh_g", [P, HID, ROWS])
        gated = sb("gated", [P, HID, ROWS])
        hT = sb("hT", [P, HID, ROWS])
        ffn = sb("ffn", [P, TILES, D])
        y = sb("y", [P, TILES, D])

        ps_x = psum("ps_x")
        ps_c = psum("ps_c")
        ps_s = psum("ps_s")
        ps_v = psum("ps_v")
        ps_h = [psum(f"ps_h{i}") for i in range(3)]
        ps_d = psum("ps_d")

        w_loaded = [sem(f"w_loaded{i}") for i in range(3)]
        g_loaded = sem("g_loaded")
        xa_loaded, xb_loaded = sem("xa_loaded"), sem("xb_loaded")
        ck_loaded, cv_loaded = sem("ck_loaded"), sem("cv_loaded")
        stored = sem("stored")
        pool_setup = sem("pool_setup")
        dve_setup = sem("dve_setup")
        consts_ready = sem("consts_ready")
        gates_ready = sem("gates_ready")
        w_cast = sem("w_cast")
        wT_in_psum = sem("wT_in_psum")
        w_ready = sem("w_ready")
        bn1_done, mom1_done, ve1_done = sem("bn1_done"), sem("mom1_done"), sem("ve1_done")
        rstd1_done, xn_done = sem("rstd1_done"), sem("xn_done")
        xT_in_psum, cT_in_psum = sem("xT_in_psum"), sem("cT_in_psum")
        xT_copied, cT_copied = sem("xT_copied"), sem("cT_copied")
        scores_done, rowmax_done, shifted_done = sem("scores_done"), sem("rowmax_done"), sem("shifted_done")
        probs_done, rowsum_done, rrec_done, coef_done = sem("probs_done"), sem("rowsum_done"), sem("rrec_done"), sem("coef_done")
        pT_in_psum, pT_copied, pv_done, pv_scaled = sem("pT_in_psum"), sem("pT_copied"), sem("pv_done"), sem("pv_scaled")
        x1_done = sem("x1_done")
        bn2_done, mom2_done, ve2_done = sem("bn2_done"), sem("mom2_done"), sem("ve2_done")
        rstd2_pow, rstd2_done, x1n_done = sem("rstd2_pow"), sem("rstd2_done"), sem("x1n_done")
        x1T_in_psum, hi_done, lo_done = sem("x1T_in_psum"), sem("hi_done"), sem("lo_done")
        gate_done, up_done = sem("gate_done"), sem("up_done")
        tanh_done, gated_done, h_done = sem("tanh_done"), sem("gated_done"), sem("h_done")
        down_done, down_scaled, y_done = sem("down_done"), sem("down_scaled"), sem("y_done")

        def has_previous(j):
            return not isinstance(j, int) or j >= 1

        def steps(engine, step, first=-3, loop_end=LOOP[1]):
            def active(c):
                return {n: 0 <= c + ahead < CHUNKS
                        for n, ahead in (("norm1", 3), ("attend", 2), ("norm2", 1), ("ffn", 0))}
            for c in range(first, LOOP[0]):
                step(c, active(c))
            with engine.Fori(LOOP[0], loop_end) as c:
                step(c, active(LOOP[0]))
            for c in range(loop_end, CHUNKS):
                step(c, active(c))

        block = stack.enter_context(nc.Block())

        @block.sync
        def _(sp):
            def load_xa(j):
                sp.dma_start(x_norm_in[:], x_rows[j]).then_inc(xa_loaded, 16)

            def load_xb(j):
                sp.dma_start(x_resid[:], x_rows[j]).then_inc(xb_loaded, 16)

            def load_ctx(dst, j, loaded):
                for u in range(2):
                    sp.dma_start(dst[64 * u:64 * u + 64], ctx_rows[j, u]).then_inc(loaded, 16)

            load_xa(0)
            load_ctx(ctx_keys, 0, ck_loaded)
            for n, w in enumerate((w_gate, w_up)):
                sp.dma_start(w_int[:, n, :].rearrange("p (k d) -> p k d", k=HID),
                             w.rearrange("(k p) d -> p k d", p=P)).then_inc(w_loaded[n], 16)
            sp.dma_start(w_int[:, 2, :], w_down).then_inc(w_loaded[2], 16)
            sp.dma_start(gates_in[:, 0:1], g_xattn.partition_broadcast(P)).then_inc(g_loaded, 16)
            sp.dma_start(gates_in[:, 1:2], g_ffn.partition_broadcast(P)).then_inc(g_loaded, 16)
            load_ctx(ctx_values, 0, cv_loaded)
            load_xb(0)
            sp.wait_ge(xn_done, 1)
            load_xa(1)

            def step(c, on):
                if on["norm1"] and not (isinstance(c, int) and (c + 4 >= CHUNKS or c == -3)):
                    sp.wait_ge(xn_done, c + 4)
                    load_xa(c + 4)
                if on["attend"] and not (isinstance(c, int) and c + 3 >= CHUNKS):
                    sp.wait_ge(cT_in_psum, c + 3)
                    load_ctx(ctx_keys, c + 3, ck_loaded)
                    sp.wait_ge(pv_done, c + 3)
                    load_ctx(ctx_values, c + 3, cv_loaded)
                    sp.wait_ge(x1_done, c + 3)
                    load_xb(c + 3)
                if on["ffn"]:
                    sp.wait_ge(y_done, c + 1)
                    sp.dma_start(out_rows[c], y[:]).then_inc(stored, 16)

            steps(sp, step, loop_end=CHUNKS - 4)
            sp.wait_ge(stored, 16 * CHUNKS)

        @block.tensor
        def _(pe):
            pe.wait_ge(pool_setup, 2)
            for n, bank in enumerate((ps_v, ps_h[0], ps_h[1])):
                pe.wait_ge(w_cast, n + 1)
                for k in range(HID):
                    mm = pe.transpose(bank[:, k * P:(k + 1) * P], w_nat[:, n, k * P:(k + 1) * P], ident[:])
                mm.then_inc(wT_in_psum, 1)

            def transposes_in(n):
                pe.wait_ge(xn_done, n + 1)
                if has_previous(n) and has_previous(n - 1):
                    pe.wait_ge(lo_done, n - 1)
                for t in range(TILES):
                    mm = pe.transpose(ps_x[:, t * P:(t + 1) * P], xn[:, t, :], ident[:])
                mm.then_inc(xT_in_psum, 1)
                pe.wait_ge(ck_loaded, 32 * (n + 1))
                if has_previous(n):
                    pe.wait_ge(pT_copied, n)
                for gh in range(TILES):
                    mm = pe.transpose(ps_c[:, gh * P:(gh + 1) * P], ctx_keys[:, gh, :], ident[:])
                mm.then_inc(cT_in_psum, 1)

            def scores(n):
                if isinstance(n, int) and n == 0:
                    pe.wait_ge(consts_ready, 1)
                    pe.wait_ge(pool_setup, 4)
                else:
                    pe.wait_ge(pv_scaled, n)
                pe.matmul(ps_s[:, 0:TILES * S], ident_bf[:], mask[:].rearrange("p t s -> p (t s)"),
                          start=True, stop=False, skip_group_check=True)
                pe.wait_ge(xT_copied, n + 1)
                pe.wait_ge(cT_copied, n + 1)
                for slot in range(TILES):
                    g, u = slot // 2, slot % 2
                    for half in range(2):
                        q0 = (2 * u + g) * P + 64 * half
                        k0 = (2 * g + half) * P + 64 * u
                        mm = pe.matmul(ps_s[64 * half:64 * half + 64, slot * S:(slot + 1) * S],
                                       xnT[:, q0:q0 + 64], ctxT[:, k0:k0 + 64],
                                       start=False, stop=True, skip_group_check=True)
                mm.then_inc(scores_done, 1)

            def probs_transposes(n):
                pe.wait_ge(probs_done, n + 1)
                for g in range(2):
                    mm = pe.transpose(ps_c[:, g * P:(g + 1) * P],
                                      probs[:, 2 * g:2 * g + 2, :].rearrange("p t s -> p (t s)"), ident[:])
                mm.then_inc(pT_in_psum, 1)

            def values(n):
                pe.wait_ge(pT_copied, n + 1)
                pe.wait_ge(cv_loaded, 32 * (n + 1))
                pe.matmul(ps_v[:, 256:258], ident_bf[:], ident_bf[:, 0:2], start=True, stop=True)
                for g in range(2):
                    for half in range(2):
                        for u in range(2):
                            dst = (ps_v[:, g * P:(g + 1) * P], ps_s[:, 256 + g * P:256 + (g + 1) * P])[u]
                            mm = pe.matmul(dst[64 * half:64 * half + 64, :],
                                           probsT[64 * u:64 * u + 64, g * P + 64 * half:g * P + 64 * half + 64],
                                           ctx_values[64 * u:64 * u + 64, 2 * g + half, :], start=True, stop=True)
                mm.then_inc(pv_done, 1)

            def transposes_mid(m):
                pe.wait_ge(x1n_done, m + 1)
                for t in range(TILES):
                    mm = pe.transpose(ps_x[:, t * P:(t + 1) * P], x1n[:, t, :], ident[:])
                mm.then_inc(x1T_in_psum, 1)

            def gate_up(c, k):
                if k == 0:
                    pe.wait_ge(lo_done, c + 1)
                elif has_previous(HID * c + k - 1):
                    pe.wait_ge(h_done, HID * c + k - 1)
                for mm_no, part in enumerate((x1T_hi, x1T_lo)):
                    mm = pe.matmul(ps_h[2 * k % 3][:], wg[:, k * P:(k + 1) * P], part[:],
                                   start=mm_no == 0, stop=mm_no == 1)
                mm.then_inc(gate_done, 1)
                if has_previous(HID * c + k):
                    pe.wait_ge(gated_done, HID * c + k)
                for mm_no, part in enumerate((x1T_hi, x1T_lo)):
                    mm = pe.matmul(ps_h[(2 * k + 1) % 3][:], wu[:, k * P:(k + 1) * P], part[:],
                                   start=mm_no == 0, stop=mm_no == 1)
                mm.then_inc(up_done, 1)

            def down(c, k):
                pe.wait_ge(h_done, HID * c + k + 1)
                if k == 0 and has_previous(c):
                    pe.wait_ge(down_scaled, c)
                for t in range(TILES):
                    mm = pe.matmul(ps_d[:, t * P:(t + 1) * P], hT[:, k, t * P:(t + 1) * P], wd[:, k, :],
                                   start=(k == 0 and t == 0), stop=(k == HID - 1), skip_group_check=True)
                if k == HID - 1:
                    mm.then_inc(down_done, 1)

            def step(c, on):
                if on["attend"]:
                    transposes_in(c + 2)
                if on["ffn"]:
                    gate_up(c, 0)
                if on["attend"]:
                    scores(c + 2)
                if on["ffn"]:
                    gate_up(c, 1)
                    down(c, 0)
                if on["attend"]:
                    probs_transposes(c + 2)
                if on["ffn"]:
                    gate_up(c, 2)
                if on["attend"]:
                    values(c + 2)
                if on["ffn"]:
                    down(c, 1)
                if on["norm2"]:
                    transposes_mid(c + 1)
                if on["ffn"]:
                    down(c, 2)

            for c in range(-3, LOOP[0]):
                if c == -1:
                    pe.wait_ge(w_ready, 3)
                step(c, dict(norm1=True, attend=c >= -2, norm2=c >= -1, ffn=c >= 0))
            with pe.Fori(*LOOP) as c:
                step(c, dict(attend=True, norm2=True, ffn=True))
            for c in range(LOOP[1], CHUNKS):
                step(c, dict(attend=c + 2 < CHUNKS, norm2=c + 1 < CHUNKS, ffn=True))

        @block.scalar
        def _(act):
            act.wait_ge(g_loaded, 32)
            act.activation(gates[:], gates_in[:], ACT.Tanh).then_inc(gates_ready, 1)
            act.wait_ge(gates_ready, 1)
            act.mul(down_scale[:], gates[:, 1:2], 0.5 * WEIGHT_SCALE ** 3).then_inc(gates_ready, 1)

            def copies_in(n):
                act.wait_ge(xT_in_psum, n + 1)
                if has_previous(n):
                    act.wait_ge(scores_done, n)
                act.copy(xnT[:], ps_x[:]).then_inc(xT_copied, 1)
                act.wait_ge(cT_in_psum, n + 1)
                act.copy(ctxT[:], ps_c[:]).then_inc(cT_copied, 1)

            def exponentials(n):
                act.wait_ge(shifted_done, n + 1)
                if has_previous(n):
                    act.wait_ge(pT_in_psum, n)
                    act.wait_ge(rowsum_done, n)
                act.activation(probs[:], shifted[:], ACT.Exp, scale=SCORE_SCALE).then_inc(probs_done, 1)

            def copy_probsT(n):
                act.wait_ge(pT_in_psum, n + 1)
                if has_previous(n):
                    act.wait_ge(pv_done, n)
                act.copy(probsT[:], ps_c[:, 0:2 * P]).then_inc(pT_copied, 1)

            def scale_values(n):
                act.wait_ge(pv_done, n + 1)
                act.wait_ge(coef_done, n + 1)
                if has_previous(n):
                    act.wait_ge(x1_done, n)
                for slot in range(TILES):
                    g, u = slot // 2, slot % 2
                    src = (ps_v[:, g * P:(g + 1) * P], ps_s[:, 256 + g * P:256 + (g + 1) * P])[u]
                    op = act.activation(attn[:, 2 * u + g, :], src, ACT.Copy, scale=coef[:, slot:slot + 1])
                op.then_inc(pv_scaled, 1)

            def normalise2(m):
                act.wait_ge(rstd2_done, m + 1)
                if has_previous(m):
                    act.wait_ge(x1T_in_psum, m)
                for t in range(TILES):
                    op = act.activation(x1n[:, t, :], x1[:, m, t, :], ACT.Identity,
                                        scale=rstd2[:, t:t + 1], bias=shift2[:, t:t + 1])
                op.then_inc(x1n_done, 1)

            def high_part(m):
                act.wait_ge(x1T_in_psum, m + 1)
                if has_previous(m):
                    act.wait_ge(up_done, HID * m)
                act.copy(x1T_hi[:], ps_x[:]).then_inc(hi_done, 1)

            def tanh_gate(c, k):
                act.wait_ge(gate_done, HID * c + k + 1)
                act.activation(tanh_g[:, k, :], ps_h[2 * k % 3][:], ACT.Tanh,
                               scale=0.5 * WEIGHT_SCALE).then_inc(tanh_done, 1)

            def scale_down(c):
                act.wait_ge(down_done, c + 1)
                if has_previous(c):
                    act.wait_ge(y_done, c)
                act.activation(ffn[:].rearrange("p t d -> p (t d)"), ps_d[:], ACT.Copy,
                               scale=down_scale[:, 0:1]).then_inc(down_scaled, 1)

            def step(c, on):
                if on["attend"]:
                    copies_in(c + 2)
                if on["ffn"]:
                    tanh_gate(c, 0)
                if on["attend"]:
                    exponentials(c + 2)
                if on["ffn"]:
                    tanh_gate(c, 1)
                if on["attend"]:
                    copy_probsT(c + 2)
                if on["ffn"]:
                    tanh_gate(c, 2)
                if on["norm2"]:
                    normalise2(c + 1)
                if on["attend"]:
                    scale_values(c + 2)
                if on["norm2"]:
                    high_part(c + 1)
                if on["ffn"]:
                    scale_down(c)

            act.wait_ge(gates_ready, 2)
            steps(act, step)

        @block.vector
        def _(dve):
            def stats(src, bn, mom, negmean, vareps, bn_done, mom_done, ve_done, j):
                for t in range(TILES):
                    op = dve.bn_stats(bn[:, t, :], src(t))
                op.then_inc(bn_done, 1)
                dve.wait_ge(bn_done, j + 1)
                dve.memset(carrier[:, 0:1], 0.0)
                for t in range(TILES):
                    op = dve.bn_aggr(mom[:, t, :], bn[:, t, :])
                op.then_inc(mom_done, 1)
                dve.wait_ge(mom_done, j + 1)
                dve.tensor_scalar(negmean[:], mom[:, :, 0], -1.0, None, ALU.mult)
                dve.tensor_scalar(vareps[:], mom[:, :, 1], EPS, None, ALU.add).then_inc(ve_done, 1)

            def stats1(j):
                dve.wait_ge(xa_loaded, 16 * (j + 1))
                if has_previous(j):
                    dve.wait_ge(xn_done, j)
                stats(lambda t: x_norm_in[:, t, :], bn1, mom1, negmean1, vareps1, bn1_done, mom1_done, ve1_done, j)

            def stats2(m):
                dve.wait_ge(x1_done, m + 1)
                if has_previous(m):
                    dve.wait_ge(rstd2_done, m)
                stats(lambda t: x1[:, m, t, :], bn2, mom2, negmean2, vareps2, bn2_done, mom2_done, ve2_done, m)

            def softmax_shift(n):
                dve.wait_ge(scores_done, n + 1)
                sc = ps_s[:, 0:TILES * S].rearrange("p (t s) -> p t s", t=TILES)
                dve.reduce_max(rowmax[:], sc, AX_X).then_inc(rowmax_done, 1)
                dve.wait_ge(rowmax_done, n + 1)
                if has_previous(n):
                    dve.wait_ge(probs_done, n)
                dve.tensor_tensor(shifted[:], sc, rowmax[:].unsqueeze(2).to_broadcast([P, TILES, S]),
                                  ALU.subtract).then_inc(shifted_done, 1)

            def softmax_sum(n):
                dve.wait_ge(probs_done, n + 1)
                dve.reduce_sum(rowsum[:], probs[:], AX_X).then_inc(rowsum_done, 1)
                dve.wait_ge(rowsum_done, n + 1)
                dve.reciprocal(rrec[:], rowsum[:]).then_inc(rrec_done, 1)
                dve.wait_ge(rrec_done, n + 1)
                if has_previous(n):
                    dve.wait_ge(pv_scaled, n)
                if isinstance(n, int) and n == 0:
                    dve.wait_ge(gates_ready, 1)
                dve.tensor_scalar(coef[:], rrec[:], gates[:, 0:1], None, ALU.mult).then_inc(coef_done, 1)

            def low_part(m):
                dve.wait_ge(hi_done, m + 1)
                dve.tensor_tensor(x1T_lo[:], ps_x[:], x1T_hi[:].bitcast(F32), ALU.subtract).then_inc(lo_done, 1)

            def gate_times(c, k):
                dve.wait_ge(tanh_done, HID * c + k + 1)
                dve.scalar_tensor_tensor(out=gated[:, k, :], in0=tanh_g[:, k, :], scalar=1.0,
                                         in1=ps_h[2 * k % 3][:], op0=ALU.add, op1=ALU.mult).then_inc(gated_done, 1)

            def up_times(c, k):
                dve.wait_ge(up_done, HID * c + k + 1)
                dve.wait_ge(gated_done, HID * c + k + 1)
                if k == 0 and has_previous(c):
                    dve.wait_ge(down_done, c)
                dve.tensor_tensor(hT[:, k, :], gated[:, k, :], ps_h[(2 * k + 1) % 3][:],
                                  ALU.mult).then_inc(h_done, 1)

            def step(c, on):
                if on["norm2"]:
                    stats2(c + 1)
                if on["ffn"]:
                    gate_times(c, 0)
                    up_times(c, 0)
                if on["attend"]:
                    softmax_shift(c + 2)
                if on["norm1"]:
                    stats1(c + 3)
                if on["ffn"]:
                    gate_times(c, 1)
                    up_times(c, 1)
                if on["attend"]:
                    softmax_sum(c + 2)
                if on["ffn"]:
                    gate_times(c, 2)
                    up_times(c, 2)
                if on["norm2"]:
                    low_part(c + 1)

            dve.wait_ge(pool_setup, 2)
            dve.tensor_copy(ident_bf[:], ident[:]).then_inc(consts_ready, 1)
            step(-3, dict(norm1=True, attend=False, norm2=False, ffn=False))
            for n in range(3):
                dve.wait_ge(w_loaded[n], 16)
                dve.tensor_copy(w_nat[:, n, :], w_int[:, n, :]).then_inc(w_cast, 1)
            for n, (dst, bank) in enumerate(((wg[:], ps_v), (wu[:], ps_h[0]),
                                             (wd[:].rearrange("p k d -> p (k d)"), ps_h[1]))):
                dve.wait_ge(wT_in_psum, n + 1)
                dve.tensor_copy(dst, bank[:, 0:H]).then_inc(w_ready, 1)
            for c in range(-2, LOOP[0]):
                step(c, dict(norm1=True, attend=True, norm2=c >= -1, ffn=c >= 0))
            with dve.Fori(*LOOP) as c:
                step(c, dict(norm1=True, attend=True, norm2=True, ffn=True))
            for c in range(LOOP[1], CHUNKS):
                step(c, dict(norm1=False, attend=c + 2 < CHUNKS, norm2=c + 1 < CHUNKS, ffn=True))

        @block.gpsimd
        def _(pool):
            pool.memset(ident[:], 0.0)
            pool.memset(minus_half[:], -0.5)
            pool.memset(mask[:], 0.0).then_inc(pool_setup, 1)
            pool.wait_ge(pool_setup, 1)
            pool.affine_select(out=ident[:], in_=ident[:], compare_op=ALU.not_equal, fill=1.0, base=0,
                               pattern=[[-1, P]], channel_multiplier=1).then_inc(pool_setup, 1)
            for half in range(2):
                pool.wait_ge(pool_setup, 2 + half)
                part = mask[64 * half:64 * half + 64]
                pool.affine_select(out=part, in_=part, compare_op=ALU.is_ge, fill=MASKED, base=0,
                                   pattern=[[0, TILES], [-1, S]], channel_multiplier=1).then_inc(pool_setup, 1)
            pool.wait_ge(pool_setup, 4)

            def norm1(j):
                if has_previous(j):
                    pool.wait_ge(xT_in_psum, j)
                pool.wait_ge(ve1_done, j + 1)
                pool.tensor_tensor(rstd1[:], vareps1[:], minus_half[:], ALU.pow).then_inc(rstd1_done, 1)
                pool.wait_ge(rstd1_done, j + 1)
                pool.tensor_tensor(carrier[:, 1:2], minus_half[:, 0:1], minus_half[:, 0:1], ALU.mult)
                for t in range(TILES):
                    op = pool.tensor_scalar(xn[:, t, :], x_norm_in[:, t, :], negmean1[:, t:t + 1],
                                            rstd1[:, t:t + 1], ALU.add, ALU.mult)
                op.then_inc(xn_done, 1)

            def add_attention(n):
                pool.wait_ge(pv_scaled, n + 1)
                pool.wait_ge(xb_loaded, 16 * (n + 1))
                pool.tensor_tensor(x1[:, n], attn[:], x_resid[:], ALU.add).then_inc(x1_done, 1)

            def rstd_of_x1(m):
                pool.wait_ge(ve2_done, m + 1)
                if has_previous(m):
                    pool.wait_ge(x1n_done, m)
                pool.tensor_tensor(rstd2[:], vareps2[:], minus_half[:], ALU.pow).then_inc(rstd2_pow, 1)
                pool.wait_ge(rstd2_pow, m + 1)
                pool.tensor_tensor(shift2[:], rstd2[:], negmean2[:], ALU.mult).then_inc(rstd2_done, 1)

            def add_ffn(c):
                pool.wait_ge(down_scaled, c + 1)
                if has_previous(c):
                    pool.wait_ge(stored, 16 * c)
                pool.tensor_tensor(y[:], ffn[:], x1[:, c], ALU.add).then_inc(y_done, 1)

            def step(c, on):
                if on["norm2"]:
                    rstd_of_x1(c + 1)
                if on["norm1"]:
                    norm1(c + 3)
                if on["attend"]:
                    add_attention(c + 2)
                if on["ffn"]:
                    add_ffn(c)

            steps(pool, step)


_INS = ["x", "ctx_1024", "g_xattn", "g_ffn", "L0_ffn_w_gate", "L0_ffn_w_up", "L0_ffn_w_down"]


def kernel(**inputs):
    import numpy as _np
    import concourse.bacc as _bacc
    from concourse import mybir as _mybir
    from concourse.bass_utils import run_bass_kernel_spmd as _run

    nc = _bacc.Bacc("TRN2", target_bir_lowering=False, num_devices=1)
    arrays, args = {}, []
    for name in _INS:
        a = _np.ascontiguousarray(inputs[name])
        arrays[f"in_{name}"] = a
        args.append(nc.dram_tensor(f"in_{name}", a.shape, _mybir.dt.from_np(a.dtype), kind="ExternalInput").ap())
    shape = arrays["in_x"].shape
    out = nc.dram_tensor("out_y", shape, _mybir.dt.float32, kind="ExternalOutput").ap()
    build(nc, *args, out)
    r = _run(nc, [arrays], core_ids=[0])
    return r.results[0]["out_y"]
```

```python
from contextlib import ExitStack

import concourse.bass as bass
from concourse import mybir

F32 = mybir.dt.float32
F32R = mybir.dt.float32r
BF16 = mybir.dt.bfloat16
I32 = mybir.dt.int32
ALU = mybir.AluOpType
ACT = mybir.ActivationFunctionType
AX_X = mybir.AxisListType.X

P = 128
EPS = 1e-5
WEIGHT_SCALE = 1.0 / 127.0
MASKED = -1e30
TILES = 4
ROWS = TILES * P
HID = 3


def build(nc, x, ctx, g_xattn, g_ffn, w_gate, w_up, w_down, out):
    B, S, D = x.shape
    H = w_gate.shape[0]
    assert D == P and S == P // 2 and H == HID * P and (B * S) % ROWS == 0
    CHUNKS = B * S // ROWS
    LOOP = (1, CHUNKS - 3)
    SCORE_SCALE = float(D) ** -0.5

    x_rows = x.rearrange("b s d -> (b s) d").rearrange("(c t p) d -> c p t d", t=TILES, p=P)
    out_rows = out.rearrange("b s d -> (b s) d").rearrange("(c t p) d -> c p t d", t=TILES, p=P)
    ctx_rows = ctx.rearrange("(c u gh) s d -> c u s gh d", u=2, gh=4)

    with ExitStack() as stack:
        def sb(name, shape, dt=F32):
            return stack.enter_context(nc.sbuf_tensor(name, shape, dt))

        def psum(name):
            return stack.enter_context(nc.psum_tensor(name, [P, 512], F32))

        def sem(name):
            return stack.enter_context(nc.semaphore(name))

        x_norm_in = sb("x_norm_in", [P, TILES, D])
        x_resid = sb("x_resid", [P, TILES, D])
        ctx_keys = sb("ctx_keys", [P, 4, D])
        ctx_values = sb("ctx_values", [P, 4, D])
        ident = sb("ident", [P, P])
        ident_bf = sb("ident_bf", [P, P], BF16)
        mask = sb("mask", [P, TILES, S], BF16)
        minus_half = sb("minus_half", [P, TILES])
        gates_in = sb("gates_in", [P, 2])
        gates = sb("gates", [P, 2])
        down_scale = sb("down_scale", [P, 1])
        carrier = sb("carrier", [P, 2])
        w_int = sb("w_int", [P, 3, H], I32)
        w_nat = sb("w_nat", [P, 3, H])
        wg = sb("wg", [P, H], F32R)
        wu = sb("wu", [P, H], F32R)
        wd = sb("wd", [P, HID, D])
        bn1 = sb("bn1", [P, TILES, 6])
        mom1 = sb("mom1", [P, TILES, 2])
        negmean1 = sb("negmean1", [P, TILES])
        vareps1 = sb("vareps1", [P, TILES])
        rstd1 = sb("rstd1", [P, TILES])
        xn = sb("xn", [P, TILES, D])
        xnT = sb("xnT", [P, ROWS])
        ctxT = sb("ctxT", [P, ROWS])
        rowmax = sb("rowmax", [P, TILES])
        shifted = sb("shifted", [P, TILES, S])
        probs = sb("probs", [P, TILES, S])
        rowsum = sb("rowsum", [P, TILES])
        rrec = sb("rrec", [P, TILES])
        coef = sb("coef", [P, TILES])
        probsT = sb("probsT", [P, 2 * P])
        x1 = sb("x1", [P, CHUNKS, TILES, D])
        bn2 = sb("bn2", [P, TILES, 6])
        mom2 = sb("mom2", [P, TILES, 2])
        negmean2 = sb("negmean2", [P, TILES])
        vareps2 = sb("vareps2", [P, TILES])
        rstd2 = sb("rstd2", [P, TILES])
        shift2 = sb("shift2", [P, TILES])
        x1n = sb("x1n", [P, TILES, D])
        x1T_hi = sb("x1T_hi", [P, ROWS], F32R)
        x1T_lo = sb("x1T_lo", [P, ROWS], F32R)
        tanh_g = sb("tanh_g", [P, HID, ROWS])
        gated = sb("gated", [P, HID, ROWS])
        hT = sb("hT", [P, HID, ROWS])
        ffn = sb("ffn", [P, TILES, D])
        y = sb("y", [P, TILES, D])

        ps_x = psum("ps_x")
        ps_c = psum("ps_c")
        ps_s = psum("ps_s")
        ps_v = psum("ps_v")
        ps_h = [psum(f"ps_h{i}") for i in range(3)]
        ps_d = psum("ps_d")

        w_loaded = [sem(f"w_loaded{i}") for i in range(3)]
        g_loaded = sem("g_loaded")
        xa_loaded, xb_loaded = sem("xa_loaded"), sem("xb_loaded")
        ck_loaded, cv_loaded = sem("ck_loaded"), sem("cv_loaded")
        stored = sem("stored")
        pool_setup = sem("pool_setup")
        dve_setup = sem("dve_setup")
        consts_ready = sem("consts_ready")
        gates_ready = sem("gates_ready")
        w_cast = sem("w_cast")
        wT_in_psum = sem("wT_in_psum")
        w_ready = sem("w_ready")
        bn1_done, mom1_done, ve1_done = sem("bn1_done"), sem("mom1_done"), sem("ve1_done")
        rstd1_done, xn_done = sem("rstd1_done"), sem("xn_done")
        xT_in_psum, cT_in_psum = sem("xT_in_psum"), sem("cT_in_psum")
        xT_copied, cT_copied = sem("xT_copied"), sem("cT_copied")
        scores_done, rowmax_done, shifted_done = sem("scores_done"), sem("rowmax_done"), sem("shifted_done")
        probs_done, rowsum_done, rrec_done, coef_done = sem("probs_done"), sem("rowsum_done"), sem("rrec_done"), sem("coef_done")
        pT_in_psum, pT_copied, pv_done = sem("pT_in_psum"), sem("pT_copied"), sem("pv_done")
        x1_done = sem("x1_done")
        bn2_done, mom2_done, ve2_done = sem("bn2_done"), sem("mom2_done"), sem("ve2_done")
        rstd2_pow, rstd2_done, x1n_done = sem("rstd2_pow"), sem("rstd2_done"), sem("x1n_done")
        x1T_in_psum, hi_done, lo_done = sem("x1T_in_psum"), sem("hi_done"), sem("lo_done")
        gate_done, up_done = sem("gate_done"), sem("up_done")
        tanh_done, gated_done, h_done = sem("tanh_done"), sem("gated_done"), sem("h_done")
        down_done, down_scaled, y_done = sem("down_done"), sem("down_scaled"), sem("y_done")

        def has_previous(j):
            return not isinstance(j, int) or j >= 1

        def steps(engine, step, first=-3, loop_end=LOOP[1]):
            def active(c):
                return {n: 0 <= c + ahead < CHUNKS
                        for n, ahead in (("norm1", 3), ("attend", 2), ("norm2", 1), ("ffn", 0))}
            for c in range(first, LOOP[0]):
                step(c, active(c))
            with engine.Fori(LOOP[0], loop_end) as c:
                step(c, active(LOOP[0]))
            for c in range(loop_end, CHUNKS):
                step(c, active(c))

        block = stack.enter_context(nc.Block())

        @block.sync
        def _(sp):
            def load_xa(j):
                sp.dma_start(x_norm_in[:], x_rows[j]).then_inc(xa_loaded, 16)

            def load_xb(j):
                sp.dma_start(x_resid[:], x_rows[j]).then_inc(xb_loaded, 16)

            def load_ctx(dst, j, loaded):
                for u in range(2):
                    sp.dma_start(dst[64 * u:64 * u + 64], ctx_rows[j, u]).then_inc(loaded, 16)

            load_xa(0)
            load_ctx(ctx_keys, 0, ck_loaded)
            for n, w in enumerate((w_gate, w_up)):
                sp.dma_start(w_int[:, n, :].rearrange("p (k d) -> p k d", k=HID),
                             w.rearrange("(k p) d -> p k d", p=P)).then_inc(w_loaded[n], 16)
            sp.dma_start(w_int[:, 2, :], w_down).then_inc(w_loaded[2], 16)
            sp.dma_start(gates_in[:, 0:1], g_xattn.partition_broadcast(P)).then_inc(g_loaded, 16)
            sp.dma_start(gates_in[:, 1:2], g_ffn.partition_broadcast(P)).then_inc(g_loaded, 16)
            load_ctx(ctx_values, 0, cv_loaded)
            load_xb(0)
            sp.wait_ge(xn_done, 1)
            load_xa(1)

            def step(c, on):
                more_keys = on["attend"] and not (isinstance(c, int) and c + 3 >= CHUNKS)
                if more_keys:
                    sp.wait_ge(cT_in_psum, c + 3)
                    load_ctx(ctx_keys, c + 3, ck_loaded)
                    sp.wait_ge(pv_done, c + 3)
                    load_ctx(ctx_values, c + 3, cv_loaded)
                if on["norm1"] and not (isinstance(c, int) and (c + 4 >= CHUNKS or c == -3)):
                    sp.wait_ge(xn_done, c + 4)
                    load_xa(c + 4)
                if more_keys:
                    sp.wait_ge(x1_done, c + 3)
                    load_xb(c + 3)
                if on["ffn"]:
                    sp.wait_ge(y_done, c + 1)
                    sp.dma_start(out_rows[c], y[:]).then_inc(stored, 16)

            steps(sp, step, loop_end=CHUNKS - 4)
            sp.wait_ge(stored, 16 * CHUNKS)

        @block.tensor
        def _(pe):
            pe.wait_ge(pool_setup, 2)
            for n, bank in enumerate((ps_v, ps_h[0], ps_h[1])):
                pe.wait_ge(w_cast, n + 1)
                for k in range(HID):
                    mm = pe.transpose(bank[:, k * P:(k + 1) * P], w_nat[:, n, k * P:(k + 1) * P], ident[:])
                mm.then_inc(wT_in_psum, 1)

            def transposes_in(n):
                pe.wait_ge(xn_done, n + 1)
                if has_previous(n) and has_previous(n - 1):
                    pe.wait_ge(lo_done, n - 1)
                for t in range(TILES):
                    mm = pe.transpose(ps_x[:, t * P:(t + 1) * P], xn[:, t, :], ident[:])
                mm.then_inc(xT_in_psum, 1)
                pe.wait_ge(ck_loaded, 32 * (n + 1))
                if has_previous(n):
                    pe.wait_ge(pT_copied, n)
                for gh in range(TILES):
                    mm = pe.transpose(ps_c[:, gh * P:(gh + 1) * P], ctx_keys[:, gh, :], ident[:])
                mm.then_inc(cT_in_psum, 1)

            def scores(n):
                if isinstance(n, int) and n == 0:
                    pe.wait_ge(consts_ready, 1)
                    pe.wait_ge(pool_setup, 4)
                else:
                    pe.wait_ge(x1_done, n)
                pe.matmul(ps_s[:, 0:TILES * S], ident_bf[:], mask[:].rearrange("p t s -> p (t s)"),
                          start=True, stop=False, skip_group_check=True)
                pe.wait_ge(xT_copied, n + 1)
                pe.wait_ge(cT_copied, n + 1)
                for slot in range(TILES):
                    g, u = slot // 2, slot % 2
                    for half in range(2):
                        q0 = (2 * u + g) * P + 64 * half
                        k0 = (2 * g + half) * P + 64 * u
                        mm = pe.matmul(ps_s[64 * half:64 * half + 64, slot * S:(slot + 1) * S],
                                       xnT[:, q0:q0 + 64], ctxT[:, k0:k0 + 64],
                                       start=False, stop=True, skip_group_check=True)
                mm.then_inc(scores_done, 1)

            def probs_transposes(n):
                pe.wait_ge(probs_done, n + 1)
                for g in range(2):
                    mm = pe.transpose(ps_c[:, g * P:(g + 1) * P],
                                      probs[:, 2 * g:2 * g + 2, :].rearrange("p t s -> p (t s)"), ident[:])
                mm.then_inc(pT_in_psum, 1)

            def values(n):
                pe.wait_ge(pT_copied, n + 1)
                pe.wait_ge(cv_loaded, 32 * (n + 1))
                pe.matmul(ps_v[:, 256:258], ident_bf[:], ident_bf[:, 0:2], start=True, stop=True)
                for g in range(2):
                    for half in range(2):
                        for u in range(2):
                            dst = (ps_v[:, g * P:(g + 1) * P], ps_s[:, 256 + g * P:256 + (g + 1) * P])[u]
                            mm = pe.matmul(dst[64 * half:64 * half + 64, :],
                                           probsT[64 * u:64 * u + 64, g * P + 64 * half:g * P + 64 * half + 64],
                                           ctx_values[64 * u:64 * u + 64, 2 * g + half, :], start=True, stop=True)
                mm.then_inc(pv_done, 1)

            def transposes_mid(m):
                pe.wait_ge(x1n_done, m + 1)
                for t in range(TILES):
                    mm = pe.transpose(ps_x[:, t * P:(t + 1) * P], x1n[:, t, :], ident[:])
                mm.then_inc(x1T_in_psum, 1)

            def twice(bank, w, k):
                for n, part in enumerate((x1T_hi, x1T_lo)):
                    mm = pe.matmul(bank[:], w[:, k * P:(k + 1) * P], part[:], start=n == 0, stop=n == 1)
                return mm

            def gate(c, k):
                if k == 0:
                    pe.wait_ge(lo_done, c + 1)
                elif has_previous(HID * c + k - 1):
                    pe.wait_ge(h_done, HID * c + k - 1)
                twice(ps_h[2 * k % 3], wg, k).then_inc(gate_done, 1)

            def up(c, k):
                if has_previous(HID * c + k):
                    pe.wait_ge(gated_done, HID * c + k)
                twice(ps_h[(2 * k + 1) % 3], wu, k).then_inc(up_done, 1)

            def down(c, k):
                pe.wait_ge(h_done, HID * c + k + 1)
                if k == 0 and has_previous(c):
                    pe.wait_ge(down_scaled, c)
                for t in range(TILES):
                    mm = pe.matmul(ps_d[:, t * P:(t + 1) * P], hT[:, k, t * P:(t + 1) * P], wd[:, k, :],
                                   start=(k == 0 and t == 0), stop=(k == HID - 1), skip_group_check=True)
                if k == HID - 1:
                    mm.then_inc(down_done, 1)

            def step(c, on):
                if on["ffn"]:
                    gate(c, 0)
                    up(c, 0)
                    gate(c, 1)
                if on["attend"]:
                    transposes_in(c + 2)
                if on["ffn"]:
                    up(c, 1)
                    down(c, 0)
                    gate(c, 2)
                if on["attend"]:
                    scores(c + 2)
                if on["ffn"]:
                    up(c, 2)
                if on["norm2"]:
                    transposes_mid(c + 1)
                if on["ffn"]:
                    down(c, 1)
                if on["attend"]:
                    probs_transposes(c + 2)
                    values(c + 2)
                if on["ffn"]:
                    down(c, 2)

            for c in range(-3, LOOP[0]):
                if c == -1:
                    pe.wait_ge(w_ready, 3)
                step(c, dict(norm1=True, attend=c >= -2, norm2=c >= -1, ffn=c >= 0))
            with pe.Fori(*LOOP) as c:
                step(c, dict(attend=True, norm2=True, ffn=True))
            for c in range(LOOP[1], CHUNKS):
                step(c, dict(attend=c + 2 < CHUNKS, norm2=c + 1 < CHUNKS, ffn=True))

        @block.scalar
        def _(act):
            act.wait_ge(g_loaded, 32)
            act.activation(gates[:], gates_in[:], ACT.Tanh).then_inc(gates_ready, 1)
            act.wait_ge(gates_ready, 1)
            act.mul(down_scale[:], gates[:, 1:2], 0.5 * WEIGHT_SCALE ** 3).then_inc(gates_ready, 1)

            def copies_in(n):
                act.wait_ge(xT_in_psum, n + 1)
                if has_previous(n):
                    act.wait_ge(scores_done, n)
                act.copy(xnT[:], ps_x[:]).then_inc(xT_copied, 1)
                act.wait_ge(cT_in_psum, n + 1)
                act.copy(ctxT[:], ps_c[:]).then_inc(cT_copied, 1)

            def exponentials(n):
                act.wait_ge(shifted_done, n + 1)
                if has_previous(n):
                    act.wait_ge(pT_in_psum, n)
                    act.wait_ge(rowsum_done, n)
                act.activation(probs[:], shifted[:], ACT.Exp, scale=SCORE_SCALE).then_inc(probs_done, 1)

            def copy_probsT(n):
                act.wait_ge(pT_in_psum, n + 1)
                if has_previous(n):
                    act.wait_ge(pv_done, n)
                act.copy(probsT[:], ps_c[:, 0:2 * P]).then_inc(pT_copied, 1)

            def normalise2(m):
                act.wait_ge(rstd2_done, m + 1)
                if has_previous(m):
                    act.wait_ge(x1T_in_psum, m)
                for t in range(TILES):
                    op = act.activation(x1n[:, t, :], x1[:, m, t, :], ACT.Identity,
                                        scale=rstd2[:, t:t + 1], bias=shift2[:, t:t + 1])
                op.then_inc(x1n_done, 1)

            def high_part(m):
                act.wait_ge(x1T_in_psum, m + 1)
                if has_previous(m):
                    act.wait_ge(up_done, HID * m)
                act.copy(x1T_hi[:], ps_x[:]).then_inc(hi_done, 1)

            def tanh_gate(c, k):
                act.wait_ge(gate_done, HID * c + k + 1)
                act.activation(tanh_g[:, k, :], ps_h[2 * k % 3][:], ACT.Tanh,
                               scale=0.5 * WEIGHT_SCALE).then_inc(tanh_done, 1)

            def scale_down(c):
                act.wait_ge(down_done, c + 1)
                if has_previous(c):
                    act.wait_ge(y_done, c)
                act.activation(ffn[:].rearrange("p t d -> p (t d)"), ps_d[:], ACT.Copy,
                               scale=down_scale[:, 0:1]).then_inc(down_scaled, 1)

            def step(c, on):
                if on["ffn"]:
                    tanh_gate(c, 0)
                    tanh_gate(c, 1)
                if on["attend"]:
                    copies_in(c + 2)
                if on["norm2"]:
                    normalise2(c + 1)
                if on["ffn"]:
                    tanh_gate(c, 2)
                if on["attend"]:
                    exponentials(c + 2)
                if on["norm2"]:
                    high_part(c + 1)
                if on["attend"]:
                    copy_probsT(c + 2)
                if on["ffn"]:
                    scale_down(c)

            act.wait_ge(gates_ready, 2)
            steps(act, step)

        @block.vector
        def _(dve):
            def bn_stats(j, src, bn, bn_done):
                for t in range(TILES):
                    op = dve.bn_stats(bn[:, t, :], src(t))
                op.then_inc(bn_done, 1)

            def bn_aggr(j, bn, bn_done, mom, mom_done):
                dve.wait_ge(bn_done, j + 1)
                dve.memset(carrier[:, 0:1], 0.0)
                for t in range(TILES):
                    op = dve.bn_aggr(mom[:, t, :], bn[:, t, :])
                op.then_inc(mom_done, 1)

            def moments(j, mom, mom_done, negmean, vareps, ve_done):
                dve.wait_ge(mom_done, j + 1)
                dve.tensor_scalar(negmean[:], mom[:, :, 0], -1.0, None, ALU.mult)
                dve.tensor_scalar(vareps[:], mom[:, :, 1], EPS, None, ALU.add).then_inc(ve_done, 1)

            def bn_stats1(j):
                dve.wait_ge(xa_loaded, 16 * (j + 1))
                bn_stats(j, lambda t: x_norm_in[:, t, :], bn1, bn1_done)

            def bn_aggr1(j):
                bn_aggr(j, bn1, bn1_done, mom1, mom1_done)

            def moments1(j):
                if has_previous(j):
                    dve.wait_ge(xn_done, j)
                moments(j, mom1, mom1_done, negmean1, vareps1, ve1_done)

            def bn_stats2(m):
                dve.wait_ge(x1_done, m + 1)
                bn_stats(m, lambda t: x1[:, m, t, :], bn2, bn2_done)

            def bn_aggr2(m):
                bn_aggr(m, bn2, bn2_done, mom2, mom2_done)

            def moments2(m):
                if has_previous(m):
                    dve.wait_ge(rstd2_done, m)
                moments(m, mom2, mom2_done, negmean2, vareps2, ve2_done)

            score_slots = ps_s[:, 0:TILES * S].rearrange("p (t s) -> p t s", t=TILES)

            def row_max(n):
                dve.wait_ge(scores_done, n + 1)
                dve.reduce_max(rowmax[:], score_slots, AX_X).then_inc(rowmax_done, 1)

            def shift(n):
                dve.wait_ge(rowmax_done, n + 1)
                if has_previous(n):
                    dve.wait_ge(probs_done, n)
                dve.tensor_tensor(shifted[:], score_slots, rowmax[:].unsqueeze(2).to_broadcast([P, TILES, S]),
                                  ALU.subtract).then_inc(shifted_done, 1)

            def row_sum(n):
                dve.wait_ge(probs_done, n + 1)
                dve.reduce_sum(rowsum[:], probs[:], AX_X).then_inc(rowsum_done, 1)

            def row_reciprocal(n):
                dve.wait_ge(rowsum_done, n + 1)
                dve.reciprocal(rrec[:], rowsum[:]).then_inc(rrec_done, 1)

            def row_coefficient(n):
                dve.wait_ge(rrec_done, n + 1)
                if isinstance(n, int) and n == 0:
                    dve.wait_ge(gates_ready, 1)
                dve.tensor_scalar(coef[:], rrec[:], gates[:, 0:1], None, ALU.mult).then_inc(coef_done, 1)

            def residual1(n):
                dve.wait_ge(pv_done, n + 1)
                dve.wait_ge(coef_done, n + 1)
                dve.wait_ge(xb_loaded, 16 * (n + 1))
                for slot in range(TILES):
                    g, u = slot // 2, slot % 2
                    src = (ps_v[:, g * P:(g + 1) * P], ps_s[:, 256 + g * P:256 + (g + 1) * P])[u]
                    op = dve.scalar_tensor_tensor(out=x1[:, n, 2 * u + g, :], in0=src, scalar=coef[:, slot:slot + 1],
                                                  in1=x_resid[:, 2 * u + g, :], op0=ALU.mult, op1=ALU.add)
                op.then_inc(x1_done, 1)

            def low_part(m):
                dve.wait_ge(hi_done, m + 1)
                dve.tensor_tensor(x1T_lo[:], ps_x[:], x1T_hi[:].bitcast(F32), ALU.subtract).then_inc(lo_done, 1)

            def gate_times(c, k):
                dve.wait_ge(tanh_done, HID * c + k + 1)
                dve.scalar_tensor_tensor(out=gated[:, k, :], in0=tanh_g[:, k, :], scalar=1.0,
                                         in1=ps_h[2 * k % 3][:], op0=ALU.add, op1=ALU.mult).then_inc(gated_done, 1)

            def up_times(c, k):
                dve.wait_ge(up_done, HID * c + k + 1)
                dve.wait_ge(gated_done, HID * c + k + 1)
                if k == 0 and has_previous(c):
                    dve.wait_ge(down_done, c)
                dve.tensor_tensor(hT[:, k, :], gated[:, k, :], ps_h[(2 * k + 1) % 3][:],
                                  ALU.mult).then_inc(h_done, 1)

            def step(c, on):
                if on["norm2"]:
                    bn_stats2(c + 1)
                    bn_aggr2(c + 1)
                if on["ffn"]:
                    gate_times(c, 0)
                if on["norm2"]:
                    moments2(c + 1)
                if on["ffn"]:
                    up_times(c, 0)
                    gate_times(c, 1)
                if on["norm1"]:
                    bn_stats1(c + 3)
                if on["ffn"]:
                    up_times(c, 1)
                if on["attend"]:
                    row_max(c + 2)
                if on["norm1"]:
                    bn_aggr1(c + 3)
                if on["attend"]:
                    shift(c + 2)
                if on["ffn"]:
                    gate_times(c, 2)
                if on["norm1"]:
                    moments1(c + 3)
                if on["attend"]:
                    row_sum(c + 2)
                if on["ffn"]:
                    up_times(c, 2)
                if on["attend"]:
                    row_reciprocal(c + 2)
                if on["norm2"]:
                    low_part(c + 1)
                if on["attend"]:
                    row_coefficient(c + 2)
                    residual1(c + 2)

            dve.wait_ge(pool_setup, 2)
            dve.tensor_copy(ident_bf[:], ident[:]).then_inc(consts_ready, 1)
            step(-3, dict(norm1=True, attend=False, norm2=False, ffn=False))
            for n in range(3):
                dve.wait_ge(w_loaded[n], 16)
                dve.tensor_copy(w_nat[:, n, :], w_int[:, n, :]).then_inc(w_cast, 1)
            for n, (dst, bank) in enumerate(((wg[:], ps_v), (wu[:], ps_h[0]),
                                             (wd[:].rearrange("p k d -> p (k d)"), ps_h[1]))):
                dve.wait_ge(wT_in_psum, n + 1)
                dve.tensor_copy(dst, bank[:, 0:H]).then_inc(w_ready, 1)
            for c in range(-2, LOOP[0]):
                step(c, dict(norm1=True, attend=True, norm2=c >= -1, ffn=c >= 0))
            with dve.Fori(*LOOP) as c:
                step(c, dict(norm1=True, attend=True, norm2=True, ffn=True))
            for c in range(LOOP[1], CHUNKS):
                step(c, dict(norm1=False, attend=c + 2 < CHUNKS, norm2=c + 1 < CHUNKS, ffn=True))

        @block.gpsimd
        def _(pool):
            pool.memset(ident[:], 0.0)
            pool.memset(minus_half[:], -0.5)
            pool.memset(mask[:], 0.0).then_inc(pool_setup, 1)
            pool.wait_ge(pool_setup, 1)
            pool.affine_select(out=ident[:], in_=ident[:], compare_op=ALU.not_equal, fill=1.0, base=0,
                               pattern=[[-1, P]], channel_multiplier=1).then_inc(pool_setup, 1)
            for half in range(2):
                pool.wait_ge(pool_setup, 2 + half)
                part = mask[64 * half:64 * half + 64]
                pool.affine_select(out=part, in_=part, compare_op=ALU.is_ge, fill=MASKED, base=0,
                                   pattern=[[0, TILES], [-1, S]], channel_multiplier=1).then_inc(pool_setup, 1)
            pool.wait_ge(pool_setup, 4)

            def norm1(j):
                if has_previous(j):
                    pool.wait_ge(xT_in_psum, j)
                pool.wait_ge(ve1_done, j + 1)
                pool.tensor_tensor(rstd1[:], vareps1[:], minus_half[:], ALU.pow).then_inc(rstd1_done, 1)
                pool.wait_ge(rstd1_done, j + 1)
                pool.tensor_tensor(carrier[:, 1:2], minus_half[:, 0:1], minus_half[:, 0:1], ALU.mult)
                for t in range(TILES):
                    op = pool.tensor_scalar(xn[:, t, :], x_norm_in[:, t, :], negmean1[:, t:t + 1],
                                            rstd1[:, t:t + 1], ALU.add, ALU.mult)
                op.then_inc(xn_done, 1)

            def rstd_of_x1(m):
                pool.wait_ge(ve2_done, m + 1)
                if has_previous(m):
                    pool.wait_ge(x1n_done, m)
                pool.tensor_tensor(rstd2[:], vareps2[:], minus_half[:], ALU.pow).then_inc(rstd2_pow, 1)
                pool.wait_ge(rstd2_pow, m + 1)
                pool.tensor_tensor(shift2[:], rstd2[:], negmean2[:], ALU.mult).then_inc(rstd2_done, 1)

            def add_ffn(c):
                pool.wait_ge(down_scaled, c + 1)
                if has_previous(c):
                    pool.wait_ge(stored, 16 * c)
                pool.tensor_tensor(y[:], ffn[:], x1[:, c], ALU.add).then_inc(y_done, 1)

            def step(c, on):
                if on["norm2"]:
                    rstd_of_x1(c + 1)
                if on["norm1"]:
                    norm1(c + 3)
                if on["ffn"]:
                    add_ffn(c)

            steps(pool, step)


_INS = ["x", "ctx_1024", "g_xattn", "g_ffn", "L0_ffn_w_gate", "L0_ffn_w_up", "L0_ffn_w_down"]


def kernel(**inputs):
    import numpy as _np
    import concourse.bacc as _bacc
    from concourse import mybir as _mybir
    from concourse.bass_utils import run_bass_kernel_spmd as _run

    nc = _bacc.Bacc("TRN2", target_bir_lowering=False, num_devices=1)
    arrays, args = {}, []
    for name in _INS:
        a = _np.ascontiguousarray(inputs[name])
        arrays[f"in_{name}"] = a
        args.append(nc.dram_tensor(f"in_{name}", a.shape, _mybir.dt.from_np(a.dtype), kind="ExternalInput").ap())
    shape = arrays["in_x"].shape
    out = nc.dram_tensor("out_y", shape, _mybir.dt.float32, kind="ExternalOutput").ap()
    build(nc, *args, out)
    r = _run(nc, [arrays], core_ids=[0])
    return r.results[0]["out_y"]
```

```python
from contextlib import ExitStack

import concourse.bass as bass
from concourse import mybir

F32 = mybir.dt.float32
F32R = mybir.dt.float32r
BF16 = mybir.dt.bfloat16
I32 = mybir.dt.int32
ALU = mybir.AluOpType
ACT = mybir.ActivationFunctionType
AX_X = mybir.AxisListType.X

P = 128
EPS = 1e-5
WEIGHT_SCALE = 1.0 / 127.0
MASKED = 1e30
TILES = 4
ROWS = TILES * P
HID = 3

WARM_START = 30
WARM_AFTER = dict(x_transposes=(4, 12), ctx_transposes=(0, 8), scores=(34, 6), probs_transposes=(2, 14), values=(12, 0))


def build(nc, x, ctx, g_xattn, g_ffn, w_gate, w_up, w_down, out):
    B, S, D = x.shape
    H = w_gate.shape[0]
    assert D == P and S == P // 2 and H == HID * P and (B * S) % ROWS == 0
    CHUNKS = B * S // ROWS
    SCORE_SCALE = float(D) ** -0.5

    x_rows = x.rearrange("b s d -> (b s) d").rearrange("(c t p) d -> c p t d", t=TILES, p=P)
    out_rows = out.rearrange("b s d -> (b s) d").rearrange("(c t p) d -> c p t d", t=TILES, p=P)
    ctx_rows = ctx.rearrange("b s d -> (b s) d").rearrange("(c t p) d -> c p t d", t=TILES, p=P)
    ctx_seqs = ctx.rearrange("(c g w h) s d -> c w h s g d", g=2, w=2, h=2)

    with ExitStack() as stack:
        def sb(name, shape, dt=F32):
            return stack.enter_context(nc.sbuf_tensor(name, shape, dt))

        def psum(name):
            return stack.enter_context(nc.psum_tensor(name, [P, 512], F32))

        def sem(name):
            return stack.enter_context(nc.semaphore(name))

        x_norm_in = sb("x_norm_in", [P, TILES, D])
        x_resid = sb("x_resid", [P, TILES, D])
        ctx_keys = sb("ctx_keys", [P, 4, D])
        ctx_values = sb("ctx_values", [P, 4, D])
        ident = sb("ident", [P, P])
        ident_bf = sb("ident_bf", [P, P], BF16)
        mask = sb("mask", [P, TILES, S], BF16)
        minus_half = sb("minus_half", [P, TILES])
        minus_one, eps = sb("minus_one", [P, TILES]), sb("eps", [P, TILES])
        gates_in = sb("gates_in", [P, 2])
        gates = sb("gates", [P, 2])
        down_scale = sb("down_scale", [P, 1])
        carrier = sb("carrier", [P, 2])
        w_int = sb("w_int", [P, 3, H], I32)
        w_nat = sb("w_nat", [P, 3, H])
        wg = sb("wg", [P, H], F32R)
        wu = sb("wu", [P, H], F32R)
        wd = sb("wd", [P, HID, D])
        bn1 = sb("bn1", [P, TILES, 6])
        mom1 = sb("mom1", [P, TILES, 2])
        negmean1 = sb("negmean1", [P, TILES])
        vareps1 = sb("vareps1", [P, TILES])
        rstd1 = sb("rstd1", [P, TILES])
        xn = sb("xn", [P, TILES, D])
        xnT = sb("xnT", [P, ROWS])
        ctxT = sb("ctxT", [P, ROWS])
        rowmin = sb("rowmin", [P, TILES])
        probs = sb("probs", [P, TILES, S])
        rowsum = sb("rowsum", [P, TILES])
        rrec = sb("rrec", [P, TILES])
        probsT = sb("probsT", [P, 2, 2 * P + 2])
        x1 = sb("x1", [P, CHUNKS, TILES, D])
        bn2 = sb("bn2", [P, TILES, 6])
        mom2 = sb("mom2", [P, TILES, 2])
        negmean2 = sb("negmean2", [P, TILES])
        vareps2 = sb("vareps2", [P, TILES])
        rstd2 = sb("rstd2", [P, TILES])
        shift2 = sb("shift2", [P, TILES])
        x1n = sb("x1n", [P, TILES, D])
        x1T_hi = sb("x1T_hi", [P, ROWS], F32R)
        x1T_lo = sb("x1T_lo", [P, ROWS], F32R)
        tanh_g = sb("tanh_g", [P, HID, ROWS])
        gated = sb("gated", [P, HID, ROWS])
        hT = sb("hT", [P, HID, ROWS])
        ffn = sb("ffn", [P, TILES, D])
        y = sb("y", [P, TILES, D])

        ps_x = psum("ps_x")
        ps_c = psum("ps_c")
        ps_v = psum("ps_v")
        ps_h = [psum(f"ps_h{i}") for i in range(4)]
        ps_d = psum("ps_d")

        w_loaded = [sem(f"w_loaded{i}") for i in range(3)]
        g_loaded = sem("g_loaded")
        x_norm_loaded, x_resid_loaded = sem("x_norm_loaded"), sem("x_resid_loaded")
        keys_loaded, values_loaded = sem("keys_loaded"), sem("values_loaded")
        stored = sem("stored")
        pool_setup = sem("pool_setup")
        probsT_zeroed = sem("probsT_zeroed")
        ident_bf_ready = sem("ident_bf_ready")
        gates_ready = sem("gates_ready")
        w_cast = sem("w_cast")
        wT_in_psum = sem("wT_in_psum")
        w_ready = sem("w_ready")
        bn1_done, mom1_done, ve1_done = sem("bn1_done"), sem("mom1_done"), sem("ve1_done")
        rstd1_done, xn_done = sem("rstd1_done"), sem("xn_done")
        xT_in_psum, cT_in_psum = sem("xT_in_psum"), sem("cT_in_psum")
        xT_copied, cT_copied = sem("xT_copied"), sem("cT_copied")
        scores_done, rowmin_done = sem("scores_done"), sem("rowmin_done")
        probs_done, rrec_done = sem("probs_done"), sem("rrec_done")
        pT_in_psum, pT_copied, pv_done = sem("pT_in_psum"), sem("pT_copied"), sem("pv_done")
        x1_done = sem("x1_done")
        x1n_dve_done = sem("x1n_dve_done")
        bn2_done, mom2_done, ve2_done = sem("bn2_done"), sem("mom2_done"), sem("ve2_done")
        rstd2_pow, rstd2_done, x1n_done = sem("rstd2_pow"), sem("rstd2_done"), sem("x1n_done")
        x1T_in_psum, hi_done, lo_done = sem("x1T_in_psum"), sem("hi_done"), sem("lo_done")
        gate_done, up_done = sem("gate_done"), sem("up_done")
        tanh_done, gated_done, h_done = sem("tanh_done"), sem("gated_done"), sem("h_done")
        down_done, down_scaled, y_done = sem("down_done"), sem("down_scaled"), sem("y_done")

        def exists(j):
            return not isinstance(j, int) or 0 <= j < CHUNKS

        def has_previous(j):
            return not isinstance(j, int) or j >= 1

        def is_last(j):
            return isinstance(j, int) and j == CHUNKS - 1

        def steps(engine, step, ahead):
            for c in range(-ahead, 1):
                step(c)
            with engine.Fori(1, CHUNKS - ahead) as c:
                step(c)
            for c in range(CHUNKS - ahead, CHUNKS):
                step(c)

        block = stack.enter_context(nc.Block())

        @block.sync
        def _(sp):
            def load_x_norm(j):
                sp.dma_start(x_norm_in[:], x_rows[j]).then_inc(x_norm_loaded, 16)

            def load_x_resid(j):
                sp.dma_start(x_resid[:], x_rows[j]).then_inc(x_resid_loaded, 16)

            def load_keys(j):
                sp.dma_start(ctx_keys[:], ctx_rows[j]).then_inc(keys_loaded, 16)

            def load_values(j):
                for u in range(2):
                    for w in range(2):
                        sp.dma_start(ctx_values[64 * u:64 * u + 64, w::2], ctx_seqs[j, w, u ^ w]).then_inc(values_loaded, 16)

            load_x_norm(0)
            load_keys(0)
            for n, w in enumerate((w_gate, w_up)):
                sp.dma_start(w_int[:, n, :].rearrange("p (k d) -> p k d", k=HID),
                             w.rearrange("(k p) d -> p k d", p=P)).then_inc(w_loaded[n], 16)
            sp.dma_start(w_int[:, 2, :], w_down).then_inc(w_loaded[2], 16)
            sp.dma_start(gates_in[:, 0:1], g_xattn.partition_broadcast(P)).then_inc(g_loaded, 16)
            sp.dma_start(gates_in[:, 1:2], g_ffn.partition_broadcast(P)).then_inc(g_loaded, 16)
            load_values(0)
            load_x_resid(0)

            def next_keys(j):
                if has_previous(j):
                    sp.wait_ge(cT_in_psum, j)
                    load_keys(j)

            def next_values(j):
                if has_previous(j):
                    sp.wait_ge(pv_done, j)
                    load_values(j)

            def next_x_norm(j):
                if has_previous(j):
                    sp.wait_ge(xn_done, j)
                    load_x_norm(j)

            def next_x_resid(j):
                if has_previous(j):
                    sp.wait_ge(x1_done, j)
                    load_x_resid(j)

            def store(j):
                sp.wait_ge(y_done, j + 1)
                sp.dma_start(out_rows[j], y[:]).then_inc(stored, 16)

            def step(c):
                if exists(c + 4):
                    next_keys(c + 4)
                if exists(c + 3):
                    next_values(c + 3)
                    next_x_resid(c + 3)
                if exists(c + 5):
                    next_x_norm(c + 5)
                if exists(c):
                    store(c)

            steps(sp, step, ahead=5)
            sp.wait_ge(stored, 16 * CHUNKS)

        @block.tensor
        def _(pe):
            def keep_warm(count):
                for _ in range(count):
                    pe.matmul(ps_d[:, 0:P], ident_bf[:], ident_bf[:], start=True, stop=True)

            def keep_warm_after(product, n):
                if isinstance(n, int) and n < 2 and product in WARM_AFTER:
                    keep_warm(WARM_AFTER[product][n])

            pe.wait_ge(ident_bf_ready, 1)
            keep_warm(WARM_START)
            pe.wait_ge(pool_setup, 2)
            for n, bank in enumerate((ps_v, ps_h[0], ps_h[1])):
                pe.wait_ge(w_cast, n + 1)
                for k in range(HID):
                    mm = pe.transpose(bank[:, k * P:(k + 1) * P], w_nat[:, n, k * P:(k + 1) * P], ident[:])
                mm.then_inc(wT_in_psum, 1)

            def x_transposes(n):
                pe.wait_ge(xn_done, n + 1)
                if has_previous(n) and has_previous(n - 1):
                    pe.wait_ge(lo_done, n - 1)
                for t in range(TILES):
                    mm = pe.transpose(ps_x[:, t * P:(t + 1) * P], xn[:, t, :], ident[:])
                mm.then_inc(xT_in_psum, 1)
                keep_warm_after("x_transposes", n)

            def ctx_transposes(n):
                pe.wait_ge(keys_loaded, 16 * (n + 1))
                if has_previous(n):
                    pe.wait_ge(probs_done, n)
                for gh in range(TILES):
                    mm = pe.transpose(ps_c[:, gh * P:(gh + 1) * P], ctx_keys[:, gh, :], ident[:])
                mm.then_inc(cT_in_psum, 1)
                keep_warm_after("ctx_transposes", n)

            def scores(n):
                if not has_previous(n):
                    pe.wait_ge(pool_setup, 4)
                pe.wait_ge(cT_copied, n + 1)
                pe.matmul(ps_c[:, 0:TILES * S], ident_bf[:], mask[:].rearrange("p t s -> p (t s)"),
                          start=True, stop=False, skip_group_check=True)
                pe.wait_ge(xT_copied, n + 1)
                for slot in range(TILES):
                    g, u = slot // 2, slot % 2
                    for half in range(2):
                        q0 = k0 = 64 * (4 * g + 2 * (u ^ half) + half)
                        mm = pe.matmul(ps_c[64 * half:64 * half + 64, slot * S:(slot + 1) * S],
                                       xnT[:, q0:q0 + 64], ctxT[:, k0:k0 + 64],
                                       start=False, stop=True, skip_group_check=True)
                mm.then_inc(scores_done, 1)
                keep_warm_after("scores", n)

            def probs_transposes(n):
                pe.wait_ge(probs_done, n + 1)
                if has_previous(n):
                    pe.wait_ge(x1_done, n)
                for g in range(2):
                    mm = pe.transpose(ps_v[:, g * P:(g + 1) * P],
                                      probs[:, 2 * g:2 * g + 2, :].rearrange("p t s -> p (t s)"), ident[:])
                mm.then_inc(pT_in_psum, 1)
                keep_warm_after("probs_transposes", n)

            def values(n):
                pe.wait_ge(pT_copied, n + 1)
                pe.wait_ge(values_loaded, 64 * (n + 1))
                for g in range(2):
                    for w in range(2):
                        lhsT = probsT[:, g, w:w + 2 * P:2]
                        mm = pe.matmul(ps_v[:, (2 * g + w) * P:(2 * g + w + 1) * P], lhsT,
                                       ctx_values[:, 2 * g + w, :], start=True, stop=True)
                mm.then_inc(pv_done, 1)
                keep_warm_after("values", n)

            def x1_transposes(m):
                pe.wait_ge(x1n_done, m + 1)
                if not has_previous(m):
                    pe.wait_ge(x1n_dve_done, 1)
                for t in range(TILES):
                    mm = pe.transpose(ps_x[:, t * P:(t + 1) * P], x1n[:, t, :], ident[:])
                mm.then_inc(x1T_in_psum, 1)

            BANK_USED = (0, -1, 1)

            def twice(bank, w, k):
                for n, part in enumerate((x1T_hi, x1T_lo)):
                    mm = pe.matmul(bank[:], w[:, k * P:(k + 1) * P], part[:], start=n == 0, stop=n == 1)
                return mm

            def gate(c, k):
                if not has_previous(c):
                    pe.wait_ge(w_ready, 3)
                if k == 0:
                    pe.wait_ge(lo_done, c + 1)
                if has_previous(c) or k > 1:
                    pe.wait_ge(gated_done, HID * c + BANK_USED[k])
                twice(ps_h[2 * k % 4], wg, k).then_inc(gate_done, 1)

            def up(c, k):
                if has_previous(c) or k > 1:
                    pe.wait_ge(h_done, HID * c + BANK_USED[k])
                twice(ps_h[(2 * k + 1) % 4], wu, k).then_inc(up_done, 1)

            def down(c, k):
                pe.wait_ge(h_done, HID * c + k + 1)
                if k == 0 and has_previous(c):
                    pe.wait_ge(down_scaled, c)
                for t in range(TILES):
                    mm = pe.matmul(ps_d[:, t * P:(t + 1) * P], hT[:, k, t * P:(t + 1) * P], wd[:, k, :],
                                   start=(k == 0 and t == 0), stop=(k == HID - 1), skip_group_check=True)
                if k == HID - 1:
                    mm.then_inc(down_done, 1)

            def step(c):
                if exists(c):
                    down(c, 2)
                if exists(c + 1):
                    gate(c + 1, 0)
                if exists(c + 3):
                    x_transposes(c + 3)
                if exists(c + 1):
                    up(c + 1, 0)
                    gate(c + 1, 1)
                if exists(c + 3):
                    scores(c + 3)
                if exists(c + 1):
                    gate(c + 1, 2)
                    up(c + 1, 1)
                    up(c + 1, 2)
                    down(c + 1, 0)
                if exists(c + 3):
                    probs_transposes(c + 3)
                if exists(c + 4):
                    ctx_transposes(c + 4)
                if exists(c + 1):
                    down(c + 1, 1)
                if exists(c + 2):
                    x1_transposes(c + 2)
                if exists(c + 3):
                    values(c + 3)

            steps(pe, step, ahead=4)

        @block.scalar
        def _(act):
            act.wait_ge(g_loaded, 32)
            act.activation(gates[:], gates_in[:], ACT.Tanh).then_inc(gates_ready, 1)
            act.wait_ge(gates_ready, 1)
            act.mul(down_scale[:], gates[:, 1:2], 0.5 * WEIGHT_SCALE ** 3).then_inc(gates_ready, 1)

            def copy_xnT(n):
                act.wait_ge(xT_in_psum, n + 1)
                if has_previous(n):
                    act.wait_ge(scores_done, n)
                act.activation(xnT[:], ps_x[:], ACT.Copy, scale=-SCORE_SCALE).then_inc(xT_copied, 1)

            def copy_ctxT(n):
                act.wait_ge(cT_in_psum, n + 1)
                if has_previous(n):
                    act.wait_ge(scores_done, n)
                act.copy(ctxT[:], ps_c[:]).then_inc(cT_copied, 1)

            def exponentials(n):
                act.wait_ge(rowmin_done, n + 1)
                if has_previous(n):
                    act.wait_ge(pT_in_psum, n)
                    act.wait_ge(rrec_done, n)
                for slot in range(TILES):
                    op = act.activation(probs[:, slot, :], ps_c[:, slot * S:(slot + 1) * S], ACT.Exp, scale=-1.0,
                                        bias=rowmin[:, slot:slot + 1], accum_out=rowsum[:, slot:slot + 1])
                op.then_inc(probs_done, 1)

            def copy_probsT(n):
                act.wait_ge(pT_in_psum, n + 1)
                if has_previous(n):
                    act.wait_ge(pv_done, n)
                else:
                    act.wait_ge(probsT_zeroed, 1)
                for u in range(2):
                    dst = (probsT[0:64].rearrange("p g (h c) -> p g h c", h=2)[:, :, :, 0:P:2],
                           probsT[64:128, :, 1:2 * P - 1].rearrange("p g (h c) -> p g h c", h=2)[:, :, :, 0:P - 1:2])[u]
                    op = act.activation(dst, ps_v[64 * u:64 * u + 64, 0:2 * P].rearrange("p (g h k) -> p g h k", g=2, h=2),
                                        ACT.Copy, scale=gates[64 * u:64 * u + 64, 0:1])
                op.then_inc(pT_copied, 1)

            def normalise2(m, half):
                if half == 0:
                    act.wait_ge(rstd2_done, m + 1)
                    if has_previous(m):
                        act.wait_ge(x1T_in_psum, m)
                if half == 1 and not has_previous(m):
                    return
                for t in range(2 * half, 2 * half + 2):
                    op = act.activation(x1n[:, t, :], x1[:, m, t, :], ACT.Identity,
                                        scale=rstd2[:, t:t + 1], bias=shift2[:, t:t + 1])
                if half == 1 or not has_previous(m):
                    op.then_inc(x1n_done, 1)

            def high_part(m):
                act.wait_ge(x1T_in_psum, m + 1)
                if has_previous(m):
                    act.wait_ge(up_done, HID * m)
                act.copy(x1T_hi[:], ps_x[:]).then_inc(hi_done, 1)

            def tanh_gate(c, k):
                act.wait_ge(gate_done, HID * c + k + 1)
                act.activation(tanh_g[:, k, :], ps_h[2 * k % 4][:], ACT.Tanh,
                               scale=0.5 * WEIGHT_SCALE).then_inc(tanh_done, 1)

            def scale_down(c):
                if is_last(c):
                    return
                act.wait_ge(down_done, c + 1)
                if has_previous(c):
                    act.wait_ge(y_done, c)
                act.activation(ffn[:].rearrange("p t d -> p (t d)"), ps_d[:], ACT.Copy,
                               scale=down_scale[:, 0:1]).then_inc(down_scaled, 1)

            act.wait_ge(gates_ready, 2)
            def step(c):
                if exists(c):
                    tanh_gate(c, 1)
                    tanh_gate(c, 2)
                if exists(c + 2):
                    exponentials(c + 2)
                if exists(c + 1):
                    normalise2(c + 1, 0)
                    normalise2(c + 1, 1)
                if exists(c + 2):
                    copy_probsT(c + 2)
                if exists(c + 1):
                    high_part(c + 1)
                if exists(c + 3):
                    copy_ctxT(c + 3)
                if exists(c + 1):
                    tanh_gate(c + 1, 0)
                if exists(c + 3):
                    copy_xnT(c + 3)
                if exists(c):
                    scale_down(c)

            steps(act, step, ahead=3)

        @block.vector
        def _(dve):
            def bn_stats(j, src, bn, bn_done):
                for t in range(TILES):
                    op = dve.bn_stats(bn[:, t, :], src(t))
                op.then_inc(bn_done, 1)

            def bn_aggr(j, bn, bn_done, mom, mom_done):
                dve.wait_ge(bn_done, j + 1)
                dve.memset(carrier[:, 0:1], 0.0)
                for t in range(TILES):
                    op = dve.bn_aggr(mom[:, t, :], bn[:, t, :])
                op.then_inc(mom_done, 1)

            def half_of_first_x1n():
                dve.wait_ge(rstd2_done, 1)
                for t in (2, 3):
                    op = dve.tensor_scalar(x1n[:, t, :], x1[:, 0, t, :], rstd2[:, t:t + 1], shift2[:, t:t + 1],
                                           ALU.mult, ALU.add)
                op.then_inc(x1n_dve_done, 1)

            def bn_stats1(j):
                dve.wait_ge(x_norm_loaded, 16 * (j + 1))
                bn_stats(j, lambda t: x_norm_in[:, t, :], bn1, bn1_done)
                if isinstance(j, int) and j == 2:
                    half_of_first_x1n()

            def bn_aggr1(j):
                if has_previous(j):
                    dve.wait_ge(ve1_done, j)
                bn_aggr(j, bn1, bn1_done, mom1, mom1_done)

            def bn_stats2(m):
                dve.wait_ge(x1_done, m + 1)
                dve.memset(carrier[:, 0:1], 0.0)
                bn_stats(m, lambda t: x1[:, m, t, :], bn2, bn2_done)

            def bn_aggr2(m):
                if has_previous(m):
                    dve.wait_ge(ve2_done, m)
                bn_aggr(m, bn2, bn2_done, mom2, mom2_done)

            score_slots = ps_c[:, 0:TILES * S].rearrange("p (t s) -> p t s", t=TILES)

            def row_minimum(n):
                dve.wait_ge(scores_done, n + 1)
                if has_previous(n):
                    dve.wait_ge(probs_done, n)
                dve.tensor_reduce(rowmin[:], score_slots, AX_X, ALU.min).then_inc(rowmin_done, 1)

            def row_reciprocal(n):
                dve.wait_ge(probs_done, n + 1)
                sums = rowsum[:].rearrange("p (g u) -> p g u", g=2)
                rec = rrec[:].rearrange("p (g w) -> p g w", g=2)
                dve.reciprocal(rec[0:64], sums[0:64])
                dve.reciprocal(rec[64:128, :, 0], sums[64:128, :, 1])
                dve.reciprocal(rec[64:128, :, 1], sums[64:128, :, 0]).then_inc(rrec_done, 1)

            def residual1(n):
                dve.wait_ge(pv_done, n + 1)
                dve.wait_ge(rrec_done, n + 1)
                dve.wait_ge(x_resid_loaded, 16 * (n + 1))
                for t in range(TILES):
                    op = dve.scalar_tensor_tensor(out=x1[:, n, t, :], in0=ps_v[:, t * P:(t + 1) * P],
                                                  scalar=rrec[:, t:t + 1], in1=x_resid[:, t, :], op0=ALU.mult, op1=ALU.add)
                op.then_inc(x1_done, 1)

            def low_part(m):
                dve.wait_ge(hi_done, m + 1)
                if has_previous(m):
                    dve.wait_ge(up_done, HID * m)
                dve.tensor_tensor(x1T_lo[:], ps_x[:], x1T_hi[:].bitcast(F32), ALU.subtract).then_inc(lo_done, 1)

            def gate_times(c, k):
                dve.wait_ge(tanh_done, HID * c + k + 1)
                dve.scalar_tensor_tensor(out=gated[:, k, :], in0=tanh_g[:, k, :], scalar=1.0,
                                         in1=ps_h[2 * k % 4][:], op0=ALU.add, op1=ALU.mult).then_inc(gated_done, 1)

            def up_times(c, k):
                dve.wait_ge(up_done, HID * c + k + 1)
                dve.wait_ge(gated_done, HID * c + k + 1)
                if k == 0 and has_previous(c):
                    dve.wait_ge(down_done, c)
                dve.tensor_tensor(hT[:, k, :], gated[:, k, :], ps_h[(2 * k + 1) % 4][:],
                                  ALU.mult).then_inc(h_done, 1)

            dve.wait_ge(pool_setup, 2)
            dve.tensor_copy(ident_bf[:], ident[:]).then_inc(ident_bf_ready, 1)
            dve.memset(probsT[:].rearrange("p g b -> p (g b)"), 0.0).then_inc(probsT_zeroed, 1)
            bn_stats1(0)
            bn_aggr1(0)
            for n in range(3):
                dve.wait_ge(w_loaded[n], 16)
                dve.tensor_copy(w_nat[:, n, :], w_int[:, n, :]).then_inc(w_cast, 1)
            dve.wait_ge(rstd1_done, 1)
            for t in range(TILES):
                op = dve.tensor_scalar(xn[:, t, :], x_norm_in[:, t, :], negmean1[:, t:t + 1],
                                       rstd1[:, t:t + 1], ALU.add, ALU.mult)
            op.then_inc(xn_done, 1)
            for n, (dst, bank) in enumerate(((wg[:], ps_v), (wu[:], ps_h[0]),
                                             (wd[:].rearrange("p k d -> p (k d)"), ps_h[1]))):
                dve.wait_ge(wT_in_psum, n + 1)
                dve.tensor_copy(dst, bank[:, 0:H]).then_inc(w_ready, 1)

            def step(c):
                if exists(c + 2):
                    row_reciprocal(c + 2)
                if exists(c):
                    up_times(c, 2)
                if exists(c + 1):
                    low_part(c + 1)
                if exists(c + 2):
                    residual1(c + 2)
                    bn_stats2(c + 2)
                if exists(c + 1):
                    gate_times(c + 1, 0)
                if exists(c + 2):
                    bn_aggr2(c + 2)
                if exists(c + 3):
                    row_minimum(c + 3)
                if exists(c + 1):
                    up_times(c + 1, 0)
                    gate_times(c + 1, 1)
                if exists(c + 4) and has_previous(c + 4):
                    bn_stats1(c + 4)
                if exists(c + 1):
                    up_times(c + 1, 1)
                if exists(c + 4) and has_previous(c + 4):
                    bn_aggr1(c + 4)
                if exists(c + 1):
                    gate_times(c + 1, 2)

            steps(dve, step, ahead=4)

            last = CHUNKS - 1
            dve.wait_ge(down_done, last + 1)
            dve.wait_ge(gates_ready, 2)
            dve.wait_ge(stored, 16 * last)
            dve.scalar_tensor_tensor(out=y[:].rearrange("p t d -> p (t d)"), in0=ps_d[:], scalar=down_scale[:, 0:1],
                                     in1=x1[:, last].rearrange("p t d -> p (t d)"),
                                     op0=ALU.mult, op1=ALU.add).then_inc(y_done, 1)

        @block.gpsimd
        def _(pool):
            pool.memset(ident[:], 0.0)
            pool.memset(minus_half[:], -0.5)
            pool.memset(minus_one[:], -1.0)
            pool.memset(eps[:], EPS)
            pool.memset(mask[:], 0.0).then_inc(pool_setup, 1)
            pool.wait_ge(pool_setup, 1)
            pool.affine_select(out=ident[:], in_=ident[:], compare_op=ALU.not_equal, fill=1.0, base=0,
                               pattern=[[-1, P]], channel_multiplier=1).then_inc(pool_setup, 1)
            for half in range(2):
                pool.wait_ge(pool_setup, 2 + half)
                part = mask[64 * half:64 * half + 64]
                pool.affine_select(out=part, in_=part, compare_op=ALU.is_ge, fill=MASKED, base=0,
                                   pattern=[[0, TILES], [-1, S]], channel_multiplier=1).then_inc(pool_setup, 1)
            pool.wait_ge(pool_setup, 4)

            def rstd_of_x(j):
                if has_previous(j):
                    pool.wait_ge(xT_in_psum, j)
                pool.wait_ge(mom1_done, j + 1)
                pool.tensor_tensor(negmean1[:], mom1[:, :, 0], minus_one[:], ALU.mult)
                pool.tensor_tensor(vareps1[:], mom1[:, :, 1], eps[:], ALU.add).then_inc(ve1_done, 1)
                pool.wait_ge(ve1_done, j + 1)
                pool.tensor_tensor(rstd1[:], vareps1[:], minus_half[:], ALU.pow).then_inc(rstd1_done, 1)

            def normalise1(j):
                if not has_previous(j):
                    return
                pool.wait_ge(rstd1_done, j + 1)
                pool.tensor_tensor(carrier[:, 1:2], minus_half[:, 0:1], minus_half[:, 0:1], ALU.mult)
                for t in range(TILES):
                    op = pool.tensor_scalar(xn[:, t, :], x_norm_in[:, t, :], negmean1[:, t:t + 1],
                                            rstd1[:, t:t + 1], ALU.add, ALU.mult)
                op.then_inc(xn_done, 1)

            def rstd_of_x1(m):
                pool.wait_ge(mom2_done, m + 1)
                if has_previous(m):
                    pool.wait_ge(x1n_done, m)
                if isinstance(m, int) and m == 1:
                    pool.wait_ge(x1n_dve_done, 1)
                pool.tensor_tensor(negmean2[:], mom2[:, :, 0], minus_one[:], ALU.mult)
                pool.tensor_tensor(vareps2[:], mom2[:, :, 1], eps[:], ALU.add).then_inc(ve2_done, 1)
                pool.wait_ge(ve2_done, m + 1)
                pool.tensor_tensor(rstd2[:], vareps2[:], minus_half[:], ALU.pow).then_inc(rstd2_pow, 1)
                pool.wait_ge(rstd2_pow, m + 1)
                pool.tensor_tensor(shift2[:], rstd2[:], negmean2[:], ALU.mult).then_inc(rstd2_done, 1)

            def add_ffn(c):
                if is_last(c):
                    return
                pool.wait_ge(down_scaled, c + 1)
                if has_previous(c):
                    pool.wait_ge(stored, 16 * c)
                pool.tensor_tensor(y[:], ffn[:], x1[:, c], ALU.add).then_inc(y_done, 1)

            def step(c):
                if exists(c + 3):
                    rstd_of_x(c + 3)
                    normalise1(c + 3)
                if exists(c + 2):
                    rstd_of_x1(c + 2)
                if exists(c):
                    add_ffn(c)

            steps(pool, step, ahead=3)


_INS = ["x", "ctx_1024", "g_xattn", "g_ffn", "L0_ffn_w_gate", "L0_ffn_w_up", "L0_ffn_w_down"]


def kernel(**inputs):
    import numpy as _np
    import concourse.bacc as _bacc
    from concourse import mybir as _mybir
    from concourse.bass_utils import run_bass_kernel_spmd as _run

    nc = _bacc.Bacc("TRN2", target_bir_lowering=False, num_devices=1)
    arrays, args = {}, []
    for name in _INS:
        a = _np.ascontiguousarray(inputs[name])
        arrays[f"in_{name}"] = a
        args.append(nc.dram_tensor(f"in_{name}", a.shape, _mybir.dt.from_np(a.dtype), kind="ExternalInput").ap())
    shape = arrays["in_x"].shape
    out = nc.dram_tensor("out_y", shape, _mybir.dt.float32, kind="ExternalOutput").ap()
    build(nc, *args, out)
    r = _run(nc, [arrays], core_ids=[0])
    return r.results[0]["out_y"]
```
